# Optimizing a Trainium2 kernel written in Bass

```python
import numpy as np
import jax
import jax.numpy as jnp

def _softmax(x, axis=-1):
    return jax.nn.softmax(x, axis=axis)

def _gelu(x):
    return jax.nn.gelu(x, approximate=True)

def _silu(x):
    return jax.nn.silu(x)

def _sigmoid(x):
    return jax.nn.sigmoid(x)

def _layernorm(x, axis=-1, eps=1e-05):
    m = jnp.mean(x, axis=axis, keepdims=True)
    v = jnp.var(x, axis=axis, keepdims=True)
    return (x - m) / jnp.sqrt(v + eps)

def _scatter_add(tgt, idx, src, axis=0):
    return tgt.at[idx].add(src)

def _segment_sum(src, seg, n):
    return jax.ops.segment_sum(src, seg, n)
kernel_name = 'mk_xattn_ffn_d2_seqx_r8_961a6f'

def setup_inputs(seed: int=0):
    np.random.seed(seed)
    _w = jnp.asarray

    def _rec_inputs():
        import jax
        import jax.numpy as jnp
        _rk = jax.random.key(seed)
        x = -0.0002928 + 1 * jax.random.normal(jax.random.fold_in(_rk, 1), (16, 128, 128), jnp.float32)
        _lenS = 128 - jax.random.randint(jax.random.fold_in(_rk, 7), (16,), 0, max(1, 128 // 4) + 1, jnp.int32)
        _lenS2 = 128 - jax.random.randint(jax.random.fold_in(_rk, 8), (16,), 0, max(1, 128 // 4) + 1, jnp.int32)
        _ctx_1024P = jax.random.normal(jax.random.fold_in(_rk, 11), (16, 16, 128), jnp.float32)
        _ctx_1024c = jax.random.dirichlet(jax.random.fold_in(_rk, 511), 0.3 * jnp.ones((16,), jnp.float32), (16, 128))
        _ctx_1024t = jnp.einsum('bsk,bkd->bsd', _ctx_1024c, _ctx_1024P)
        _ctx_1024t = _ctx_1024t * jax.lax.rsqrt(jnp.mean(jnp.square(_ctx_1024t)) + 1e-12) * 0.953939
        ctx_1024 = -1.39393e-06 + 0.999914 * (_ctx_1024t + 0.3 * jax.random.normal(jax.random.fold_in(_rk, 611), (16, 128, 128), jnp.float32))
        fside_BxSxS2_0 = jax.random.uniform(jax.random.fold_in(_rk, 12), (16, 128, 128), jnp.float32, 0.0, 1)
        _validS = jnp.arange(128)[None, :] < _lenS[:, None]
        _validS2 = jnp.arange(128)[None, :] < _lenS2[:, None]
        _causal = jnp.tril(jnp.ones((128, 128), dtype=bool))
        mask_BxSxS2_ik1 = jnp.where(jnp.broadcast_to(_validS2[:, None, :], (16, 128, 128)), 1, 0).astype(jnp.int32)
        return (x, ctx_1024, fside_BxSxS2_0, mask_BxSxS2_ik1)
    x, ctx_1024, fside_BxSxS2_0, mask_BxSxS2_ik1 = _rec_inputs()

    def _L0_xattn_setup():
        import jax, jax.numpy as jnp
        import numpy as np
        NUM_HEADS = 16
        HIDDEN = 128
        B, S = (2, 256)

        def _split_heads(x, H):
            b, s, d = x.shape
            return x.reshape(b, s, H, d // H).transpose(0, 2, 1, 3)
        key = jax.random.key(seed)
        ks = jax.random.split(key, 14)
        D = HIDDEN
        scale = 1.0 / np.sqrt(D)
        inp = {'query': jax.random.normal(ks[0], (B, S, D), jnp.float32), 'key_in': jax.random.normal(ks[1], (B, S, D), jnp.float32), 'value': jax.random.normal(ks[2], (B, S, D), jnp.float32), 'group_prob': jax.random.uniform(ks[3], (B, S, S), jnp.float32), 'mask': jax.random.randint(ks[4], (B, S, S), 0, 2, jnp.int32), 'wq_k': jax.random.normal(ks[5], (D, D), jnp.float32) * scale, 'wq_b': jnp.zeros((D,), jnp.float32), 'wk_k': jax.random.normal(ks[6], (D, D), jnp.float32) * scale, 'wk_b': jnp.zeros((D,), jnp.float32), 'wv_k': jax.random.normal(ks[7], (D, D), jnp.float32) * scale, 'wv_b': jnp.zeros((D,), jnp.float32), 'wo_k': jax.random.normal(ks[8], (D, D), jnp.float32) * scale, 'wo_b': jnp.zeros((D,), jnp.float32)}
        return inp
    _L0_xattn_all = _L0_xattn_setup()
    _L0_xattn_in = {k: v for k, v in _L0_xattn_all.items() if k in ('wq_k', 'wq_b', 'wk_k', 'wk_b', 'wv_k', 'wv_b', 'wo_k', 'wo_b')}
    del _L0_xattn_all

    def _L0_ffn_setup():
        import jax, jax.numpy as jnp
        import numpy as np
        HIDDEN = 128
        INNER = 512

        def _weight_quant(w):
            scale = 1.0 / jnp.clip(jnp.mean(jnp.abs(w)), 1e-05)
            wq = jnp.clip(jnp.round(w * scale), -1.0, 1.0) / scale
            return w + jax.lax.stop_gradient(wq - w)

        def _act_quant(x):
            scale = 127.0 / jnp.clip(jnp.max(jnp.abs(x), axis=-1, keepdims=True), 1e-05)
            xq = jnp.clip(jnp.round(x * scale), -128.0, 127.0) / scale
            return x + jax.lax.stop_gradient(xq - x)

        def _bitlinear(x, w):
            return jnp.einsum('bsi,oi->bso', _act_quant(x), _weight_quant(w))
        key = jax.random.key(seed)
        k0, k1, k2, k3 = jax.random.split(key, 4)
        x = jax.random.normal(k0, (4, 256, HIDDEN), dtype=jnp.float32)
        w_gate = jax.random.normal(k1, (INNER, HIDDEN), dtype=jnp.float32) / np.sqrt(HIDDEN)
        w_up = jax.random.normal(k2, (INNER, HIDDEN), dtype=jnp.float32) / np.sqrt(HIDDEN)
        w_down = jax.random.normal(k3, (HIDDEN, INNER), dtype=jnp.float32) / np.sqrt(INNER)
        return {'x': x, 'w_gate': w_gate, 'w_up': w_up, 'w_down': w_down}
    _L0_ffn_all = _L0_ffn_setup()
    _L0_ffn_in = {k: v for k, v in _L0_ffn_all.items() if k in ('w_gate', 'w_up', 'w_down')}
    del _L0_ffn_all

    def _L1_xattn_setup():
        import jax, jax.numpy as jnp
        import numpy as np
        DIM = 128
        NUM_HEADS = 16
        DIM_HEAD = 64
        INNER = NUM_HEADS * DIM_HEAD
        SCALE = DIM_HEAD ** (-0.5)

        def _layernorm(x, gamma, beta, eps=1e-05):
            mu = jnp.mean(x, axis=-1, keepdims=True)
            var = jnp.mean(jnp.square(x - mu), axis=-1, keepdims=True)
            return (x - mu) * jax.lax.rsqrt(var + eps) * gamma + beta
        key = jax.random.key(seed)
        ks = jax.random.split(key, 8)
        B, SQ, SK = (2, 256, 512)
        x = jax.random.normal(ks[0], (B, SQ, DIM), dtype=jnp.float32)
        context = jax.random.normal(ks[1], (B, SK, DIM), dtype=jnp.float32)
        ln_gamma = jnp.ones((DIM,), jnp.float32)
        ln_beta = jnp.zeros((DIM,), jnp.float32)
        w_q = jax.random.normal(ks[2], (DIM, INNER), dtype=jnp.float32) / np.sqrt(DIM)
        w_kv = jax.random.normal(ks[3], (DIM, 2 * INNER), dtype=jnp.float32) / np.sqrt(DIM)
        w_out = jax.random.normal(ks[4], (INNER, DIM), dtype=jnp.float32) / np.sqrt(INNER)
        b_out = jnp.zeros((DIM,), jnp.float32)
        gate = jnp.array([0.5], jnp.float32)
        return {'x': x, 'context': context, 'ln_gamma': ln_gamma, 'ln_beta': ln_beta, 'w_q': w_q, 'w_kv': w_kv, 'w_out': w_out, 'b_out': b_out, 'gate': gate}
    _L1_xattn_all = _L1_xattn_setup()
    _L1_xattn_in = {k: v for k, v in _L1_xattn_all.items() if k in ('ln_gamma', 'ln_beta', 'w_q', 'w_kv', 'w_out', 'b_out', 'gate')}
    del _L1_xattn_all

    def _L1_ffn_setup():
        import jax, jax.numpy as jnp
        import numpy as np
        from jax import lax
        DIM = 128
        HID = 256
        E = 8
        K = 2
        B, T = (2, 64)
        key = jax.random.key(seed)
        ks = jax.random.split(key, 5)
        scale = 1.0 / np.sqrt(DIM)
        x = jax.random.normal(ks[0], (B, T, DIM), dtype=jnp.float32)
        router_w = jax.random.normal(ks[1], (E, DIM), dtype=jnp.float32) * scale
        w_gate = jax.random.normal(ks[2], (E, HID, DIM), dtype=jnp.float32) * scale
        w_up = jax.random.normal(ks[3], (E, HID, DIM), dtype=jnp.float32) * scale
        w_down = jax.random.normal(ks[4], (E, DIM, HID), dtype=jnp.float32) * (1.0 / np.sqrt(HID))
        return {'x': x, 'router_w': router_w, 'w_gate': w_gate, 'w_up': w_up, 'w_down': w_down}
    _L1_ffn_all = _L1_ffn_setup()
    _L1_ffn_in = {k: v for k, v in _L1_ffn_all.items() if k in ('router_w', 'w_gate', 'w_up', 'w_down')}
    del _L1_ffn_all
    return {'x': x, 'ctx_1024': ctx_1024, 'fside_BxSxS2_0': fside_BxSxS2_0, 'mask_BxSxS2_ik1': mask_BxSxS2_ik1, 'L0_xattn_wq_k': _L0_xattn_in['wq_k'], 'L0_xattn_wq_b': _L0_xattn_in['wq_b'], 'L0_xattn_wk_k': _L0_xattn_in['wk_k'], 'L0_xattn_wk_b': _L0_xattn_in['wk_b'], 'L0_xattn_wv_k': _L0_xattn_in['wv_k'], 'L0_xattn_wv_b': _L0_xattn_in['wv_b'], 'L0_xattn_wo_k': _L0_xattn_in['wo_k'], 'L0_xattn_wo_b': _L0_xattn_in['wo_b'], 'L0_ffn_w_gate': _L0_ffn_in['w_gate'], 'L0_ffn_w_up': _L0_ffn_in['w_up'], 'L0_ffn_w_down': _L0_ffn_in['w_down'], 'L1_xattn_ln_gamma': _L1_xattn_in['ln_gamma'], 'L1_xattn_ln_beta': _L1_xattn_in['ln_beta'], 'L1_xattn_w_q': _L1_xattn_in['w_q'], 'L1_xattn_w_kv': _L1_xattn_in['w_kv'], 'L1_xattn_w_out': _L1_xattn_in['w_out'], 'L1_xattn_b_out': _L1_xattn_in['b_out'], 'L1_xattn_gate': _L1_xattn_in['gate'], 'L1_ffn_router_w': _L1_ffn_in['router_w'], 'L1_ffn_w_gate': _L1_ffn_in['w_gate'], 'L1_ffn_w_up': _L1_ffn_in['w_up'], 'L1_ffn_w_down': _L1_ffn_in['w_down']}

def reference(x, ctx_1024, fside_BxSxS2_0, mask_BxSxS2_ik1, L0_xattn_wq_k, L0_xattn_wq_b, L0_xattn_wk_k, L0_xattn_wk_b, L0_xattn_wv_k, L0_xattn_wv_b, L0_xattn_wo_k, L0_xattn_wo_b, L0_ffn_w_gate, L0_ffn_w_up, L0_ffn_w_down, L1_xattn_ln_gamma, L1_xattn_ln_beta, L1_xattn_w_q, L1_xattn_w_kv, L1_xattn_w_out, L1_xattn_b_out, L1_xattn_gate, L1_ffn_router_w, L1_ffn_w_gate, L1_ffn_w_up, L1_ffn_w_down):
    import jax
    import jax.numpy as jnp

    def _L0_xattn_ref(query, key_in, value, group_prob, mask, wq_k, wq_b, wk_k, wk_b, wv_k, wv_b, wo_k, wo_b):
        import jax, jax.numpy as jnp
        import numpy as np
        NUM_HEADS = 16
        HIDDEN = 128
        B, S = (2, 256)

        def _split_heads(x, H):
            b, s, d = x.shape
            return x.reshape(b, s, H, d // H).transpose(0, 2, 1, 3)
        H = NUM_HEADS
        dh = query.shape[-1] // H
        q = _split_heads(query @ wq_k + wq_b, H)
        k = _split_heads(key_in @ wk_k + wk_b, H)
        v = _split_heads(value @ wv_k + wv_b, H)
        logits = jnp.einsum('bhqd,bhkd->bhqk', q, k) / jnp.sqrt(jnp.asarray(dh, q.dtype))
        neg = (1.0 - mask.astype(q.dtype)) * -1000000000.0
        logits = logits + neg[:, None, :, :]
        attn = jax.nn.softmax(logits, axis=-1)
        attn = attn * group_prob[:, None, :, :]
        out = jnp.einsum('bhqk,bhkd->bhqd', attn, v)
        out = out.transpose(0, 2, 1, 3).reshape(query.shape[0], -1, H * dh)
        return out @ wo_k + wo_b

    def _L0_ffn_ref(x, w_gate, w_up, w_down):
        import jax, jax.numpy as jnp
        import numpy as np
        HIDDEN = 128
        INNER = 512

        def _weight_quant(w):
            scale = 1.0 / jnp.clip(jnp.mean(jnp.abs(w)), 1e-05)
            wq = jnp.clip(jnp.round(w * scale), -1.0, 1.0) / scale
            return w + jax.lax.stop_gradient(wq - w)

        def _act_quant(x):
            scale = 127.0 / jnp.clip(jnp.max(jnp.abs(x), axis=-1, keepdims=True), 1e-05)
            xq = jnp.clip(jnp.round(x * scale), -128.0, 127.0) / scale
            return x + jax.lax.stop_gradient(xq - x)

        def _bitlinear(x, w):
            return jnp.einsum('bsi,oi->bso', _act_quant(x), _weight_quant(w))
        gate = jax.nn.silu(_bitlinear(x, w_gate))
        up = _bitlinear(x, w_up)
        return _bitlinear(gate * up, w_down)

    def _L1_xattn_ref(x, context, ln_gamma, ln_beta, w_q, w_kv, w_out, b_out, gate):
        import jax, jax.numpy as jnp
        import numpy as np
        DIM = 128
        NUM_HEADS = 16
        DIM_HEAD = 64
        INNER = NUM_HEADS * DIM_HEAD
        SCALE = DIM_HEAD ** (-0.5)

        def _layernorm(x, gamma, beta, eps=1e-05):
            mu = jnp.mean(x, axis=-1, keepdims=True)
            var = jnp.mean(jnp.square(x - mu), axis=-1, keepdims=True)
            return (x - mu) * jax.lax.rsqrt(var + eps) * gamma + beta
        B, SQ, _ = x.shape
        SK = context.shape[1]
        xn = _layernorm(x, ln_gamma, ln_beta)
        q = (xn @ w_q).reshape(B, SQ, NUM_HEADS, DIM_HEAD)
        kv = context @ w_kv
        k, v = jnp.split(kv, 2, axis=-1)
        k = k.reshape(B, SK, NUM_HEADS, DIM_HEAD)
        v = v.reshape(B, SK, NUM_HEADS, DIM_HEAD)
        scores = jnp.einsum('bqhd,bkhd->bhqk', q * SCALE, k)
        attn = jax.nn.softmax(scores, axis=-1)
        out = jnp.einsum('bhqk,bkhd->bqhd', attn, v).reshape(B, SQ, INNER)
        out = out @ w_out + b_out
        return out * jnp.tanh(gate[0])

    def _L1_ffn_ref(x, router_w, w_gate, w_up, w_down):
        import jax, jax.numpy as jnp
        import numpy as np
        from jax import lax
        DIM = 128
        HID = 256
        E = 8
        K = 2
        B, T = (2, 64)
        Bb, Tt, D = x.shape
        N = Bb * Tt
        xf = x.reshape(N, D)
        logits = xf @ router_w.T
        routing = jax.nn.softmax(logits, axis=-1)
        top_w, top_i = lax.top_k(routing, K)
        top_w = top_w / jnp.sum(top_w, axis=-1, keepdims=True)
        combine = jnp.zeros((N, E), dtype=x.dtype)
        combine = combine.at[jnp.arange(N)[:, None], top_i].add(top_w)
        g = jnp.einsum('nd,ehd->neh', xf, w_gate)
        u = jnp.einsum('nd,ehd->neh', xf, w_up)
        h = jax.nn.silu(g) * u
        y = jnp.einsum('neh,edh->ned', h, w_down)
        out = jnp.einsum('ned,ne->nd', y, combine)
        return out.reshape(Bb, Tt, D)
    x = x + _L0_xattn_ref(_layernorm(x, axis=-1), ctx_1024, ctx_1024, fside_BxSxS2_0, mask_BxSxS2_ik1, L0_xattn_wq_k, L0_xattn_wq_b, L0_xattn_wk_k, L0_xattn_wk_b, L0_xattn_wv_k, L0_xattn_wv_b, L0_xattn_wo_k, L0_xattn_wo_b)
    x = x + _L0_ffn_ref(_layernorm(x, axis=-1), L0_ffn_w_gate, L0_ffn_w_up, L0_ffn_w_down)
    x = x + _L1_xattn_ref(_layernorm(x, axis=-1), ctx_1024, L1_xattn_ln_gamma, L1_xattn_ln_beta, L1_xattn_w_q, L1_xattn_w_kv, L1_xattn_w_out, L1_xattn_b_out, L1_xattn_gate)
    x = x + _L1_ffn_ref(_layernorm(x, axis=-1), L1_ffn_router_w, L1_ffn_w_gate, L1_ffn_w_up, L1_ffn_w_down)
    return x

_drawn_inputs = setup_inputs


def setup_inputs(seed=0):
    import zlib

    import numpy as np

    out = dict(_drawn_inputs(seed))
    spreads = {'L0_xattn_wq_b': (0.0, 0.1),
     'L0_xattn_wk_b': (0.0, 0.1),
     'L0_xattn_wv_b': (0.0, 0.1),
     'L0_xattn_wo_b': (0.0, 0.1),
     'L1_xattn_ln_gamma': (1.0, 0.2),
     'L1_xattn_ln_beta': (0.0, 0.1),
     'L1_xattn_b_out': (0.0, 0.1)}
    factors = {}
    for name, (base, spread) in spreads.items():
        noise = np.random.default_rng([zlib.crc32(name.encode()), seed]).standard_normal(out[name].shape)
        drawn = base * np.exp(spread * noise) if base else spread * noise
        out[name] = jnp.asarray(drawn.astype(out[name].dtype))
    for name, factor in factors.items():
        out[name] = (out[name] * factor).astype(out[name].dtype)
    return out
```

```python
from contextlib import ExitStack

import concourse.bass as bass
from concourse import mybir

F32 = mybir.dt.float32
F32R = mybir.dt.float32r
BF16 = mybir.dt.bfloat16
I32 = mybir.dt.int32
ALU = mybir.AluOpType
ACT = mybir.ActivationFunctionType
AX_X = mybir.AxisListType.X

P = 128
NB = 16
GB = 4
NG = NB // GB
T = GB * P
H = 16
D0 = P // H
D1 = 64
INNER1 = H * D1
C1 = INNER1 // P
HG = 4
NHG = H // HG
UNITS0 = GB * NHG
F0 = 512
CF = F0 // P
E = 8
HID = 256
CE = HID // P
NCH = E * CE
TOPK = 2
SLOTS = 6
EPS = 1e-5
MASKED = 1e9
MAGIC = 12582912.0
Q_PARTS = (0, 0, 0, 1, 1, 1, 2, 2)
K_PARTS = (0, 1, 2, 0, 1, 2, 0, 1)
TERMS = len(Q_PARTS)


def heads_of(i):
    return [2 * (HG * (i // 2) + n) + i % 2 for n in range(HG)]


class Event:

    def __init__(self, sem, n):
        self.sem, self.n, self.made = sem, n, 0

    def at(self, g, k=1):
        return g * self.n + k

    def on(self, ins, by=1):
        self.made += by
        return ins.then_inc(self.sem, by)


class Ring:

    def __init__(self, banks, units, read_by):
        self.banks, self.units, self.read_by = banks, units, read_by
        self.at = {u: n for n, u in enumerate(units)}
        assert len(self.at) == len(units)

    def bank(self, unit):
        return self.banks[self.at[unit] % len(self.banks)]

    def wait_free(self, pe, unit, g):
        n = self.at[unit] - len(self.banks)
        if n >= 0:
            event, k = self.read_by(self.units[n])
            pe.wait_ge(event.sem, event.at(g, k))


def attention_steps(u):
    return [("T", u)] + [("S", u + 2)] * (u + 2 < UNITS0) + [("O", u - 1)] * (u > 0)


ATTENTION_START = [("S", 0), ("S", 1)]
ALL_ATTENTION = ATTENTION_START + [s for u in range(UNITS0) for s in attention_steps(u)] + [("O", UNITS0 - 1)]


def chunk_steps(c, side):
    h = 2 * c + side
    ahead = c + 2 < C1
    return ([("T", h)] + [("Q", c + 2), ("K", c + 2)] * (side and ahead) + [("S", h + 2)] * (h + 2 < H)
            + [("O", h - 1)] * (h > 0) + ([("A", c - 1)] * (c > 0) if side else [("W", c - 2)] * (c > 1)))


CHUNK_START = [("Q", 0), ("K", 0), ("Q", 1), ("K", 1), ("S", 0), ("S", 1)]
CHUNK_END = [("O", H - 1), ("W", C1 - 2), ("A", C1 - 1), ("W", C1 - 1)]
ALL_CHUNKS = CHUNK_START + [s for c in range(C1) for side in range(2) for s in chunk_steps(c, side)] + CHUNK_END

A_SLOTS = ([("norm", 3), ("turn", 4), ("project", 25), ("attend_start", 6)]
           + [(("attend", u), 5) for u in range(UNITS0)]
           + [("combine", 6), ("quant", 7), ("turn_quant", 2)] + [(("ffn", j, i), 3) for j in range(GB) for i in range(2)])
B_SLOTS = ([("norm", 7), ("turn", 3), ("project", 9), ("chunk_start", 6)]
           + [(("chunk", c, side), 6) for c in range(C1) for side in range(2)]
           + [("combine", 3), ("turn_out", 3), ("norm_x3", 4), ("turn_x3", 4), ("route", 7)]
           + [(("expert", n, i), 2) for n in range(NCH) for i in range(2)] + [("finish", 4)])
ROUNDS = (C1 + NCH) // 2
ROUND_SLOTS = [(r, 1) for r in range(ROUNDS)]


def merged(*sequences):
    out = []
    for n, (name, slots) in enumerate(sequences):
        total, at = sum(w for _, w in slots), 0
        for k, (slot, w) in enumerate(slots):
            out.append((at / total, n, k, name, slot))
            at += w
    return [(name, slot) for *_, name, slot in sorted(out, key=lambda o: o[:3])]

N_CONSTANTS = 11
SET_UP = 5
A_STEPS, B_STEPS = 52, 42


def two_layers(nc, x, ctxT, gp_dram, mask, wq, bq, wk, bk, wv, bv, wo, bo, fwgT, fwuT, fwdT,
               gamma, beta, wv1, bout1, gate, routerT, chunks,
               identity, expert_selector, earlier, out):
    stack = ExitStack()
    with stack:
        def sb(name, shape, dt=F32):
            return stack.enter_context(nc.sbuf_tensor(name, shape, dt))

        def sem(name):
            return stack.enter_context(nc.semaphore(name))

        events = {}

        def event(name, n=1):
            events[name] = Event(sem(name), n)
            return events[name]

        def pair(name, n):
            return sb(name + "_hi", [P, n], F32R), sb(name + "_lo", [P, n], F32R)

        ident = sb("ident", [P, P])
        ident_b = sb("ident_b", [P, P], BF16)
        expert_sel = sb("expert_sel", [3 * E, E * P], BF16)
        lt = sb("lt", [P, E * E])
        ones = sb("ones", [P, P])
        minus_half = sb("minus_half", [P, GB])
        w_q, w_k, w_v, w_o = (pair(n, P) for n in ("w_q", "w_k", "w_v", "w_o"))
        w_v1 = pair("w_v1", INNER1)
        w_r = pair("w_r", E)
        w_slot = sb("w_slot", [P, SLOTS, 2, 3, P], F32R)
        fw_g, fw_u, fw_d = (sb(n, [P, F0], BF16) for n in ("fw_g", "fw_u", "fw_d"))
        f_sum = sb("f_sum", [P, 3])
        f_mean = sb("f_mean", [P, 3])
        f_inv = sb("f_inv", [P, 3])
        f_c = sb("f_c", [P, 3])
        bq_c, bk_c, bo1_c, gate_c, tanh_gate, bo1_g, bq_s = (
            sb(n, [P, 1]) for n in ("bq_c", "bk_c", "bo1_c", "gate_c", "tanh_gate", "bo1_g", "bq_s"))
        bv_b, bo_b, gamma_b, beta_b = (sb(n, [P, P]) for n in ("bv_b", "bo_b", "gamma_b", "beta_b"))

        xa = sb("xa", [P, GB, P])
        ca = sb("ca", [P, T])
        gp = sb("gp", [P, GB, P])
        mk = sb("mk", [P, GB, P], I32)
        neg = sb("neg", [P, GB, P], BF16)
        a_st, a_mv, a_ve, a_rs = sb("a_st", [P, GB, 6]), sb("a_mv", [P, GB, 2]), sb("a_ve", [P, GB]), sb("a_rs", [P, GB])
        a_xc, a_n = sb("a_xc", [P, GB, P]), sb("a_n", [P, GB, P])
        a_t = pair("a_t", T)
        a_c = pair("a_c", T)
        qk_3 = [sb("q_3", [P, 3, T], BF16), sb("k_3", [P, 3, T], BF16)]
        qk_r = sb("qk_r", [P, T])
        q_st = sb("q_st", [P, H // 2, T], BF16)
        k_st = sb("k_st", [P, H // 2, T], BF16)
        va = sb("va", [P, GB, P])
        a_nm, a_sum = sb("a_nm", [P, 4, HG]), sb("a_sum", [P, 2, H])
        a_p = [sb(f"a_p{i}", [P, HG, P]) for i in range(2)]
        a_g = [sb(f"a_g{i}", [P, HG, P]) for i in range(2)]
        a_gT = [sb(f"a_gT{i}", [P, HG * P]) for i in range(2)]
        flat = lambda b: b[:, :, :].rearrange("p h n -> p (h n)")
        qk_f = th = [flat(b) for b in a_p]
        hid = [flat(b) for b in a_g]
        a_rd = sb("a_rd", [P, H])
        att = sb("att", [P, GB, P])
        x1 = sb("x1", [P, GB, P])
        x2 = sb("x2", [P, GB, P])
        mx, s127, s_half, s_up, s_both = (sb(n, [P, GB]) for n in ("mx", "s127", "s_half", "s_up", "s_both"))
        mh, h127, s_down = (sb(n, [P, GB]) for n in ("mh", "h127", "s_down"))
        qx = sb("qx", [P, GB, P])
        qxT = sb("qxT", [P, T], BF16)
        hqT = [sb(f"hqT{i}", [P, CF * P], BF16) for i in range(2)]

        xb = sb("xb", [P, GB, P])
        cb = sb("cb", [P, T])
        b_st, b_mv, b_ve, b_rs = sb("b_st", [P, GB, 6]), sb("b_mv", [P, GB, 2]), sb("b_ve", [P, GB]), sb("b_rs", [P, GB])
        b_xc, b_n = sb("b_xc", [P, GB, P]), sb("b_n", [P, GB, P])
        b_t = pair("b_t", T)
        b_c = pair("b_c", T)
        qk1 = sb("qk1", [P, 4, T])
        q1T, k1T = ([qk1[:, 2 * n + i, :] for i in range(2)] for n in range(2))
        round_in = [qk1[:, :, :].rearrange("p a b -> p (a b)")[:, i * 6 * P:(i + 1) * 6 * P].rearrange(
            "p (c m n) -> p c m n", c=2, m=3) for i in range(2)]
        v1 = sb("v1", [P, GB, H, D1])
        b_nm, b_sum = sb("b_nm", [P, 4, GB]), sb("b_sum", [P, 4, GB])
        b_p = [sb(f"b_p{i}", [P, GB, P]) for i in range(2)]
        b_pT = [sb(f"b_pT{i}", [P, T]) for i in range(2)]
        b_rd = sb("b_rd", [P, 4, GB])
        att1 = [sb(f"att1_{i}", [P, GB, P]) for i in range(2)]
        x3 = sb("x3", [P, GB, P])
        lg, sel, cw = sb("lg", [P, GB, E]), sb("sel", [P, GB, E]), sb("cw", [P, GB, E])
        red, red2 = sb("red", [P, GB]), sb("red2", [P, GB])
        above, same = sb("above", [P, GB, E, E]), sb("same", [P, GB, E, E])
        cr = sb("cr", [P, GB, E])
        c3 = sb("c3", [P, GB, 3, E], BF16)
        c3T = sb("c3T", [3 * E, T], BF16)
        work = sb("work", [P, 8 * T])
        c_b, tg, hf, yc = ([work[:, (2 * n + i) * T:(2 * n + i + 1) * T] for i in range(2)] for n in range(4))
        hp = [pair(f"hp{i}", T) for i in range(2)]
        acc = sb("acc", [P, T])
        xo = sb("xo", [P, GB, P])

        bank = [stack.enter_context(nc.psum_tensor(f"bank{i}", [P, 512], F32)) for i in range(8)]
        yT = acc
        chunks_dram = nc.dram_tensor("chunks_in_parts", [C1 + NCH, P, 6 * P], F32).ap()
        stacked_dram = [nc.dram_tensor(n, [H, TERMS, D0, T], BF16).ap() for n in ("q_stacked", "k_stacked")]

        x_in, ctx_in, gp_in, mask_in, ctxb_in, out_done = (
            event(n, k) for n, k in (("x_in", 16), ("ctx_in", 16), ("gp_in", 16), ("mask_in", 16),
                                     ("ctxb_in", 16), ("out_done", 16)))
        parts_out, stack_in = event("parts_out", 2 * 16 * TERMS), event("stack_in", 4 * 16)
        a_var, a_rstd, a_normed = event("a_var", 2), event("a_rstd", 2), event("a_normed")
        a_turned, a_hi, a_lo = event("a_turned", 3), event("a_hi", 2), event("a_lo", 2)
        a_chi, a_clo = event("a_chi"), event("a_clo")
        a_projected, a_qk, a_split, a_v, a_masks = (
            event("a_projected", 3), event("a_qk", 2), event("a_split", 2), event("a_v"), event("a_masks"))
        a_scored, a_max, a_exp, a_weighted, a_gturned, a_gT_in, a_summed = (
            event(n, UNITS0) for n in ("a_scored", "a_max", "a_exp", "a_weighted", "a_gturned", "a_gT_in", "a_summed"))
        a_attended, a_wo_done, a_wo_read = event("a_attended", GB), event("a_wo_done"), event("a_wo_read")
        a_scales, a_quant, a_quantT = event("a_scales"), event("a_quant"), event("a_quantT")
        a_gate_up, a_tanh, a_gated, a_hidden = (event("a_gate_up", 2 * GB), event("a_tanh", GB),
                                                event("a_gated", GB), event("a_hidden", GB))
        a_hquant, a_hturned, a_hT, a_down, a_out = (
            event(n, GB) for n in ("a_hquant", "a_hturned", "a_hT", "a_down", "a_out"))

        b_var, b_rstd, b_normed = event("b_var", 3), event("b_rstd", 3), event("b_normed", 2)
        b_turned, b_hi, b_lo = event("b_turned", 4), event("b_hi", 2), event("b_lo", 2)
        b_chi, b_clo = event("b_chi"), event("b_clo")
        b_q_done, b_k_done, b_q, b_k = (event(n, C1) for n in ("b_q_done", "b_k_done", "b_q", "b_k"))
        w_come = [event(f"w_come{i}", 16 * (C1 + NCH) // SLOTS) for i in range(SLOTS)]
        b_v_done, b_v = event("b_v_done", 2 * GB), event("b_v", 2 * GB)
        b_scored, b_max, b_exp, b_pturned, b_pT_in, b_summed, b_attended = (
            event(n, H) for n in ("b_scored", "b_max", "b_exp", "b_pturned", "b_pT_in", "b_summed", "b_attended"))
        b_aturned, b_ahi, b_alo, b_wout = (event(n, C1) for n in ("b_aturned", "b_ahi", "b_alo", "b_wout"))
        b_gated_out, b_x3 = event("b_gated_out"), event("b_x3")
        b_logits, b_lshift, b_lexp, b_combine, b_cturned, b_cT = (
            event(n) for n in ("b_logits", "b_lshift", "b_lexp", "b_combine", "b_cturned", "b_cT"))
        b_g, b_u, b_tanh, b_gated, b_hidden, b_hhi, b_hlo, b_y = (
            event(n, NCH) for n in ("b_g", "b_u", "b_tanh", "b_gated", "b_hidden", "b_hhi", "b_hlo", "b_y"))
        b_cspread, b_cin, b_ycomb = event("b_cspread", E), event("b_cin", E), event("b_ycomb", E)
        b_acc, b_out = event("b_acc", E - 1), event("b_out")
        a_step, b_step = event("a_step", A_STEPS), event("b_step", B_STEPS)
        consts_in, small_in, f_in, hi_made, set_up, f_summed, f_total, s_set, group_met, round_hi, round_lo = (
            sem(n) for n in ("consts_in", "small_in", "f_in", "hi_made", "set_up", "f_summed",
                             "f_total", "s_set", "group_met", "round_hi", "round_lo"))
        round_come, round_out = ([sem(f"{n}{i}") for i in range(2)] for n in ("round_come", "round_out"))

        def a_read(u):
            if u in ("xT", "attT"):
                return a_lo, 1 + (u == "attT")
            if u in ("q", "k"):
                return a_qk, 1 + (u == "k")
            if u in ("v", "wo", "qxT"):
                return {"v": a_v, "wo": a_wo_read, "qxT": a_quantT}[u], 1
            kind, j = u[0], u[1]
            return {"S": a_exp, "T": a_gT_in, "g": a_gated, "u": a_hidden, "h": a_hT}[kind], j + 1

        def b_read(u):
            if u in ("xT", "x3T"):
                return b_lo, 1 + (u == "x3T")
            if u in ("x3", "lg", "cT", "fin"):
                return {"x3": b_x3, "lg": b_lshift, "cT": b_cT, "fin": b_out}[u], 1
            kind, j = u[0], u[1]
            if kind == "v":
                return b_v, 2 * j + u[2] + 1
            return {"S": b_exp, "T": b_pT_in, "Q": b_q, "K": b_k, "A": b_alo, "g": b_gated, "u": b_hidden,
                    "c": b_cin}[kind], j + 1

        banked = [s for s in ALL_ATTENTION if s[0] != "O"]
        ffn_units = [("g", 0), ("u", 0)]
        for j in range(GB):
            ffn_units.append(("h", j))
            if j + 1 < GB:
                ffn_units += [("g", j + 1), ("u", j + 1)]
        expert_units = [("g", 0), ("u", 0)]
        for n in range(NCH):
            if n % CE == CE - 1:
                expert_units.append(("c", n // CE))
            if n + 1 < NCH:
                expert_units += [("g", n + 1), ("u", n + 1)]
        ring_a = Ring(bank[0:2], ["xT", "q", "k", "v"] + banked + ["attT", "wo", "qxT"] + ffn_units, a_read)
        chunk_units = [s for s in ALL_CHUNKS if s[0] not in "OW"]
        ring_b = Ring(bank[3:6], ["xT"] + [("v", j, n) for j in range(GB) for n in range(2)] + chunk_units
                      + ["x3", "x3T", "lg", "cT"] + expert_units + ["fin"], b_read)
        values_a, values_b = bank[2][:, 0:P], bank[6][:, 0:GB * D1]
        sums_b = bank[7]

        tiles = lambda ap: ap.rearrange("p (j n) -> p j n", n=P)
        spread = lambda ap, n: ap.unsqueeze(len(ap.shape)).to_broadcast(list(ap.shape) + [n])
        over_tiles = lambda ap: ap.unsqueeze(1).to_broadcast([P, GB, ap.shape[1]])
        rows_of = lambda dram, g: dram[bass.ds(g * GB, GB)].rearrange("b s d -> s b d")
        of = lambda j, n=P: slice(j * n, (j + 1) * n)

        SMALL = [(wq, w_q), (wk, w_k), (wv, w_v), (wo, w_o), (routerT, w_r), (wv1, w_v1)]
        FFN = [(fwgT, fw_g), (fwuT, fw_u), (fwdT, fw_d)]
        small_at, at = [], 0
        for src in [w[0] for w in SMALL + FFN]:
            small_at.append(work[:, at:at + src.shape[1]])
            at += src.shape[1]
        f_at = small_at[len(SMALL):]
        slots_of = lambda r: w_slot[:, 2 * (r % 2):2 * (r % 2) + 2]

        def weight(i, part):
            return w_slot[:, i % SLOTS, 0, part, :], w_slot[:, i % SLOTS, 1, part, :]

        def run(eng, a, b, set_up_round=None):
            def one_pass(n, slots):
                if eng is nc.sync:
                    if not isinstance(n, int) or n:
                        eng.wait_ge(group_met, 5 * n)
                for layer, slot in slots:
                    if layer == "first":
                        a(n, slot)
                    elif layer == "second":
                        b(n - 1, slot)
                    elif set_up_round:
                        set_up_round(slot)
                if eng is nc.sync:
                    eng.sem_inc(group_met, 1)
                else:
                    eng.drain().then_inc(group_met, 1)
                    eng.wait_ge(group_met, 5 * n + 5)

            one_pass(0, merged(("first", A_SLOTS), ("rounds", ROUND_SLOTS)))
            with eng.Fori(1, NG) as g:
                one_pass(g, merged(("first", A_SLOTS), ("second", B_SLOTS)))
            one_pass(NG, merged(("second", B_SLOTS)))

        expert_sel_f = k_st[0:3 * E, :, :].rearrange("p a b -> p (a b)").bitcast(F32)[:, 0:E * P]

        block = stack.enter_context(nc.Block())

        @block.sync
        def _(sp):
            constants = [(ident[:, :], identity), (expert_sel_f, expert_selector), (lt[:, :], earlier.to_broadcast([P, E * E])),
                         (bq_c[:, :], bq), (bk_c[:, :], bk), (bo1_c[:, :], bout1),
                         (gate_c[:, :], gate.to_broadcast([P, 1])), (bv_b[:, :], bv.to_broadcast([P, P])),
                         (bo_b[:, :], bo.to_broadcast([P, P])), (gamma_b[:, :], gamma.to_broadcast([P, P])),
                         (beta_b[:, :], beta.to_broadcast([P, P]))]
            assert len(constants) == N_CONSTANTS
            for dst, src in constants:
                sp.dma_start(dst, src).then_inc(consts_in, 16)
            for (src, _), dst in zip(SMALL, small_at):
                sp.dma_start(dst, src).then_inc(small_in, 16)
            for (src, _), dst in zip(FFN, f_at):
                sp.dma_start(dst, src).then_inc(f_in, 16)

            def round_load(r):
                sp.dma_start(round_in[r % 2][:, :, :, :].rearrange("p c m n -> p c (m n)"),
                             chunks[2 * r:2 * r + 2].rearrange("c p n -> p c n")).then_inc(round_come[r % 2], 16)

            def set_up_round(r):
                if r == 0:
                    round_load(0)
                    round_load(1)
                sp.wait_ge(round_lo, r + 1)
                sp.dma_start(chunks_dram[2 * r:2 * r + 2].rearrange("c p n -> p c n"),
                             slots_of(r).rearrange("p c h m n -> p c (h m n)").bitcast(F32)).then_inc(round_out[r % 2], 16)
                if r + 2 < ROUNDS:
                    round_load(r + 2)
                if r == ROUNDS - 1:
                    for i in range(2):
                        sp.wait_ge(round_out[i], 16 * ROUNDS // 2)

            def a(g, s):
                if s == "norm":
                    x_in.on(sp.dma_start(xa[:, :, :], rows_of(x, g)), 16)
                    ctx_in.on(sp.dma_start(ca[:, :], ctxT[:, bass.ds(g * T, T)]), 16)
                    mask_in.on(sp.dma_start(mk[:, :, :], rows_of(mask, g)), 16)
                    gp_in.on(sp.dma_start(gp[:, :, :], rows_of(gp_dram, g)), 16)
                elif s == "project":
                    for n, terms in enumerate((Q_PARTS, K_PARTS)):
                        sp.wait_ge(a_split.sem, a_split.at(g, n + 1))
                        for t, part in enumerate(terms):
                            parts_out.on(sp.dma_start(stacked_dram[n][:, t], qk_3[n][:, part, :]), 16)
                    sp.wait_ge(parts_out.sem, parts_out.at(g, 2 * 16 * TERMS))
                    for n, dst in enumerate((q_st, k_st)):
                        for side in range(2):
                            src = stacked_dram[n].rearrange("(j s) c d t -> s (c d) j t", s=2)[side]
                            stack_in.on(sp.dma_start(dst[64 * side:64 * side + 64, :, :], src), 16)

            def b(g, s):
                def chunk(i):
                    w_come[i % SLOTS].on(sp.dma_start(
                        w_slot[:, i % SLOTS].rearrange("p h m n -> p (h m n)").bitcast(F32), chunks_dram[i]), 16)

                if s == "norm":
                    ctxb_in.on(sp.dma_start(cb[:, :], ctxT[:, bass.ds(g * T, T)]), 16)
                    for i in range(SLOTS):
                        chunk(i)
                elif s[0] == "chunk" and s[1] >= 2 and s[2] == 1:
                    sp.wait_ge(b_wout.sem, b_wout.at(g, s[1] - 1))
                    chunk(s[1] - 2 + SLOTS)
                elif s == "combine":
                    for c in (C1 - 2, C1 - 1):
                        sp.wait_ge(b_wout.sem, b_wout.at(g, c + 1))
                        chunk(c + SLOTS)
                elif s[0] == "expert" and s[2] == 0 and s[1] >= 2 and s[1] - 2 + SLOTS < NCH:
                    sp.wait_ge(b_y.sem, b_y.at(g, s[1] - 1))
                    chunk(C1 + s[1] - 2 + SLOTS)
                elif s == "finish":
                    sp.wait_ge(b_out.sem, b_out.at(g))
                    out_done.on(sp.dma_start(rows_of(out, g), xo[:, :, :]), 16)
                    sp.wait_ge(out_done.sem, out_done.at(g, 16))

            run(sp, a, b, set_up_round)

        @block.tensor
        def _(pe):
            mm = nc.tensor.matmul

            def product(dst, left, right, start=True, stop=True):
                (lh, ll), (rh, rl) = left, right
                mm(dst, lh, rh, start=start, stop=False)
                mm(dst, lh, rl, start=False, stop=False)
                return mm(dst, ll, rh, start=False, stop=stop)

            def cols(w, s):
                return w[0][:, s], w[1][:, s]

            def turn(dst, src):
                for j in range(GB):
                    last = nc.tensor.transpose(dst[:, of(j)], src[:, j, :], ident[:, :])
                return last

            pe.wait_ge(f_summed, 1)
            mm(bank[0][:, 0:3], ones[:, :], f_sum[:, :], start=True, stop=True).then_inc(f_total, 1)
            pe.wait_ge(set_up, SET_UP)

            def attend(g, steps):
                for kind, u in steps:
                    j, heads = u // NHG, heads_of(u % NHG)
                    if kind != "O":
                        ring_a.wait_free(pe, (kind, u), g)
                        dst = ring_a.bank((kind, u))
                    if kind == "S":
                        mm(dst[:, :].rearrange("p (h n) -> p h n", h=HG), ident_b[:, :],
                           neg[:, j:j + 1, :].to_broadcast([P, HG, P]), start=True, stop=False, skip_group_check=True)
                        for n, h in enumerate(heads):
                            rows, slot = slice(64 * (h % 2), 64 * (h % 2) + 64), h // 2
                            last = mm(dst[:, of(n)], q_st[rows, slot, of(j)], k_st[rows, slot, of(j)],
                                      start=False, stop=n == HG - 1, skip_group_check=True)
                        a_scored.on(last)
                    elif kind == "T":
                        pe.wait_ge(a_weighted.sem, a_weighted.at(g, u + 1))
                        a_gturned.on(turn(dst, a_g[u % 2]))
                    else:
                        pe.wait_ge(a_gT_in.sem, a_gT_in.at(g, u + 1))
                        if u % NHG == 0 and j:
                            pe.wait_ge(a_attended.sem, a_attended.at(g, j))
                        for n, h in enumerate(heads):
                            last = mm(values_a[:, of(h, D0)], a_gT[u % 2][:, of(n)], va[:, j, of(h, D0)],
                                      start=True, stop=True)
                        a_summed.on(last)

            def come(g, i):
                e = w_come[i % SLOTS]
                pe.wait_ge(e.sem, e.at(g, 16 * (i // SLOTS + 1)))

            def chunk_step(g, s):
                kind, c = s[0], s[1]
                if kind not in "OW":
                    ring_b.wait_free(pe, s, g)
                    dst = ring_b.bank(s)
                if kind == "Q":
                    come(g, c)
                    b_q_done.on(product(dst[:, :], weight(c, 0), cols(b_t, of(0, T))))
                elif kind == "K":
                    b_k_done.on(product(dst[:, :], weight(c, 1), cols(b_c, of(0, T))))
                elif kind == "S":
                    h = c
                    c, half = h // 2, of(h % 2, D1)
                    pe.wait_ge(b_q.sem, b_q.at(g, c + 1))
                    pe.wait_ge(b_k.sem, b_k.at(g, c + 1))
                    for j in range(GB):
                        last = mm(dst[:, of(j)], q1T[c % 2][half, of(j)], k1T[c % 2][half, of(j)], start=True, stop=True)
                    b_scored.on(last)
                elif kind == "T":
                    h = c
                    pe.wait_ge(b_exp.sem, b_exp.at(g, h + 1))
                    b_pturned.on(turn(dst, b_p[h % 2]))
                elif kind == "O":
                    h = c
                    pe.wait_ge(b_pT_in.sem, b_pT_in.at(g, h + 1))
                    if h:
                        pe.wait_ge(b_attended.sem, b_attended.at(g, h))
                    for j in range(GB):
                        last = mm(values_b[:, of(j, D1)], b_pT[h % 2][:, of(j)], v1[:, j, h, :], start=True, stop=True)
                    b_summed.on(last)
                elif kind == "A":
                    pe.wait_ge(b_attended.sem, b_attended.at(g, 2 * c + 2))
                    b_aturned.on(turn(dst, att1[c % 2]))
                else:
                    pe.wait_ge(b_alo.sem, b_alo.at(g, c + 1))
                    b_wout.on(product(sums_b[:, :], weight(c, 2), cols(hp[c % 2], of(0, T)),
                                      start=c == 0, stop=c == C1 - 1))

            def a(g, s):
                if s == "turn":
                    pe.wait_ge(a_normed.sem, a_normed.at(g))
                    a_turned.on(turn(ring_a.bank("xT"), a_n))
                elif s == "project":
                    ring_a.wait_free(pe, "q", g)
                    pe.wait_ge(a_lo.sem, a_lo.at(g, 1))
                    a_projected.on(product(ring_a.bank("q")[:, :], cols(w_q, of(0)), cols(a_t, of(0, T))))
                    ring_a.wait_free(pe, "k", g)
                    pe.wait_ge(a_clo.sem, a_clo.at(g))
                    a_projected.on(product(ring_a.bank("k")[:, :], cols(w_k, of(0)), cols(a_c, of(0, T))))
                    ring_a.wait_free(pe, "v", g)
                    for j in range(GB):
                        last = product(ring_a.bank("v")[:, of(j)], cols(a_c, of(j)), cols(w_v, of(0)))
                    a_projected.on(last)
                elif s == "attend_start":
                    pe.wait_ge(stack_in.sem, stack_in.at(g, 4 * 16))
                    pe.wait_ge(a_masks.sem, a_masks.at(g))
                    pe.wait_ge(a_v.sem, a_v.at(g))
                    attend(g, ATTENTION_START)
                elif s[0] == "attend":
                    attend(g, attention_steps(s[1]))
                elif s == "combine":
                    attend(g, [("O", UNITS0 - 1)])
                    ring_a.wait_free(pe, "attT", g)
                    pe.wait_ge(a_attended.sem, a_attended.at(g, GB))
                    a_turned.on(turn(ring_a.bank("attT"), att))
                    ring_a.wait_free(pe, "wo", g)
                    pe.wait_ge(a_lo.sem, a_lo.at(g, 2))
                    for j in range(GB):
                        last = product(ring_a.bank("wo")[:, of(j)], cols(a_t, of(j)), cols(w_o, of(0)))
                    a_wo_done.on(last)
                elif s == "turn_quant":
                    ring_a.wait_free(pe, "qxT", g)
                    pe.wait_ge(a_quant.sem, a_quant.at(g))
                    a_turned.on(turn(ring_a.bank("qxT"), qx))
                elif s[0] == "ffn":
                    def gate_up(j):
                        for n, w in (("g", fw_g), ("u", fw_u)):
                            ring_a.wait_free(pe, (n, j), g)
                            a_gate_up.on(mm(ring_a.bank((n, j))[:, :], qxT[:, of(j)], w[:, :], start=True, stop=True))

                    j = s[1]
                    if s == ("ffn", 0, 0):
                        pe.wait_ge(a_quantT.sem, a_quantT.at(g))
                        gate_up(0)
                    elif s[2]:
                        ring_a.wait_free(pe, ("h", j), g)
                        pe.wait_ge(a_hquant.sem, a_hquant.at(g, j + 1))
                        for c in range(CF):
                            last = nc.tensor.transpose(ring_a.bank(("h", j))[:, of(c)], hid[j % 2][:, of(c)], ident[:, :])
                        a_hturned.on(last)
                        if j + 1 < GB:
                            gate_up(j + 1)
                        pe.wait_ge(a_hT.sem, a_hT.at(g, j + 1))
                        if j:
                            pe.wait_ge(a_out.sem, a_out.at(g, j))
                        for c in range(CF):
                            last = mm(values_a, hqT[j % 2][:, of(c)], fw_d[:, of(c)],
                                      start=c == 0, stop=c == CF - 1)
                        a_down.on(last)

            def down(g, n):
                pe.wait_ge(b_hlo.sem, b_hlo.at(g, n + 1))
                if n % CE == 0 and n:
                    pe.wait_ge(b_ycomb.sem, b_ycomb.at(g, n // CE))
                b_y.on(product(sums_b[:, :], weight(C1 + n, 2), cols(hp[n % 2], of(0, T)),
                               start=n % CE == 0, stop=n % CE == CE - 1))

            def b(g, s):
                if s == "turn":
                    pe.wait_ge(b_normed.sem, b_normed.at(g, 1))
                    b_turned.on(turn(ring_b.bank("xT"), b_n))
                elif s == "project":
                    pe.wait_ge(b_lo.sem, b_lo.at(g, 1))
                    pe.wait_ge(b_clo.sem, b_clo.at(g))
                    for j in range(GB):
                        for n in range(2):
                            ring_b.wait_free(pe, ("v", j, n), g)
                            b_v_done.on(product(ring_b.bank(("v", j, n))[:, :], cols(b_c, of(j)), cols(w_v1, of(n, 512))))
                elif s == "chunk_start":
                    for step in CHUNK_START:
                        chunk_step(g, step)
                elif s[0] == "chunk":
                    if s[1:] == (0, 0):
                        pe.wait_ge(b_v.sem, b_v.at(g, 2 * GB))
                    for step in chunk_steps(s[1], s[2]):
                        chunk_step(g, step)
                elif s == "combine":
                    for step in CHUNK_END:
                        chunk_step(g, step)
                elif s == "turn_out":
                    ring_b.wait_free(pe, "x3", g)
                    pe.wait_ge(b_gated_out.sem, b_gated_out.at(g))
                    b_turned.on(turn(ring_b.bank("x3"), tiles(yT[:, :])))
                elif s == "turn_x3":
                    ring_b.wait_free(pe, "x3T", g)
                    pe.wait_ge(b_normed.sem, b_normed.at(g, 2))
                    b_turned.on(turn(ring_b.bank("x3T"), b_n))
                    ring_b.wait_free(pe, "lg", g)
                    pe.wait_ge(b_lo.sem, b_lo.at(g, 2))
                    for j in range(GB):
                        last = product(ring_b.bank("lg")[:, of(j, E)], cols(b_t, of(j)), cols(w_r, of(0, E)))
                    b_logits.on(last)
                elif s[0] == "expert":
                    n = s[1]

                    def gate_up(n):
                        come(g, C1 + n)
                        for part, (kind, done) in enumerate((("g", b_g), ("u", b_u))):
                            ring_b.wait_free(pe, (kind, n), g)
                            done.on(product(ring_b.bank((kind, n))[:, :], weight(C1 + n, part), cols(b_t, of(0, T))))

                    e = n // CE
                    if s[2] == 0:
                        if n == 0:
                            ring_b.wait_free(pe, "cT", g)
                            pe.wait_ge(b_combine.sem, b_combine.at(g))
                            turned = ring_b.bank("cT")[0:3 * E, 0:T // 2].bitcast(BF16)
                            for j in range(GB):
                                last = nc.tensor.transpose(
                                    turned[:, of(j)], c3[:, j, :, :].rearrange("p c e -> p (c e)"), ident_b[:, :])
                            b_cturned.on(last)
                            gate_up(0)
                        if n % CE == CE - 1:
                            ring_b.wait_free(pe, ("c", e), g)
                            pe.wait_ge(b_cT.sem, b_cT.at(g))
                            b_cspread.on(mm(ring_b.bank(("c", e))[:, :], expert_sel[:, of(e)], c3T[:, :],
                                            start=True, stop=True))
                        if n + 1 < NCH:
                            gate_up(n + 1)
                    elif n:
                        down(g, n - 1)
                elif s == "finish":
                    down(g, NCH - 1)
                    ring_b.wait_free(pe, "fin", g)
                    pe.wait_ge(b_acc.sem, b_acc.at(g, E - 1))
                    b_turned.on(turn(ring_b.bank("fin"), tiles(acc[:, :])))

            run(pe, a, b)

        @block.scalar
        def _(act):
            act.wait_ge(consts_in, 16 * N_CONSTANTS)
            act.wait_ge(small_in, 16 * len(SMALL))
            for (_, w), src in zip(SMALL, small_at):
                nc.scalar.copy(w[0][:, :], src).then_inc(hi_made, 1)
            nc.scalar.activation(tanh_gate[:, :], gate_c[:, :], ACT.Tanh).then_inc(s_set, 1)
            act.wait_ge(s_set, 1)
            nc.scalar.mul(bo1_g[:, :], bo1_c[:, :], tanh_gate[:, 0:1]).then_inc(set_up, 1)
            nc.scalar.mul(bq_s[:, :], bq_c[:, :], D0 ** -0.5).then_inc(set_up, 1)
            def set_up_round(r):
                act.wait_ge(round_come[r % 2], 16 * (r // 2 + 1))
                if r >= 2:
                    act.wait_ge(round_out[r % 2], 16 * (r // 2))
                nc.scalar.copy(slots_of(r)[:, :, 0].rearrange("p c m n -> p c (m n)"),
                               round_in[r % 2][:, :, :, :].rearrange("p c m n -> p c (m n)")).then_inc(round_hi, 1)

            act.wait_ge(set_up, SET_UP)

            def exponential(g, src, u, maxima, exp, p, nm, sums, read):
                act.wait_ge(maxima.sem, maxima.at(g, u + 1))
                if u >= 2:
                    act.wait_ge(read.sem, read.at(g, u - 1))
                for n in range(4):
                    last = nc.scalar.activation(p[:, n, :], src[:, of(n)], ACT.Exp, bias=nm[:, n:n + 1],
                                                accum_out=sums[n])
                exp.on(last)

            def exp_a(g, u):
                j = u // NHG
                exponential(g, ring_a.bank(("S", u)), u, a_max, a_exp, a_p[u % 2], a_nm[:, u % 4, :],
                            [a_sum[:, j % 2, h:h + 1] for h in heads_of(u % NHG)], a_weighted)

            def exp_b(g, h):
                exponential(g, ring_b.bank(("S", h)), h, b_max, b_exp, b_p[h % 2], b_nm[:, h % 4, :],
                            [b_sum[:, h % 4, j:j + 1] for j in range(GB)], b_pturned)

            def turned_in_b(g, h):
                act.wait_ge(b_pturned.sem, b_pturned.at(g, h + 1))
                if h >= 2:
                    act.wait_ge(b_summed.sem, b_summed.at(g, h - 1))
                b_pT_in.on(nc.scalar.copy(b_pT[h % 2][:, :], ring_b.bank(("T", h))[:, :]))

            def query(g, c):
                act.wait_ge(b_q_done.sem, b_q_done.at(g, c + 1))
                b_q.on(nc.scalar.mul(q1T[c % 2], ring_b.bank(("Q", c))[:, :], D1 ** -0.5))

            def attended_hi(g, c):
                act.wait_ge(b_aturned.sem, b_aturned.at(g, c + 1))
                if c >= 2:
                    act.wait_ge(b_wout.sem, b_wout.at(g, c - 1))
                b_ahi.on(nc.scalar.copy(hp[c % 2][0][:, :], ring_b.bank(("A", c))[:, :]))

            def a(g, s):
                if s == "norm":
                    act.wait_ge(ctx_in.sem, ctx_in.at(g, 16))
                    a_chi.on(nc.scalar.copy(a_c[0][:, :], ca[:, :]))
                elif s == "turn":
                    act.wait_ge(a_turned.sem, a_turned.at(g, 1))
                    a_hi.on(nc.scalar.copy(a_t[0][:, :], ring_a.bank("xT")[:, :]))
                elif s == "project":
                    for n, (name, scale, bias) in enumerate((("q", D0 ** -0.5, bq_s), ("k", 1.0, bk_c))):
                        act.wait_ge(a_projected.sem, a_projected.at(g, n + 1))
                        a_qk.on(nc.scalar.activation(qk_f[n], ring_a.bank(name)[:, :], ACT.Identity,
                                                     bias=bias[:, 0:1], scale=scale))
                elif s == "attend_start":
                    for u in range(2):
                        exp_a(g, u)
                elif s[0] == "attend" and s[1] + 2 < UNITS0:
                    exp_a(g, s[1] + 2)
                elif s == "combine":
                    act.wait_ge(a_turned.sem, a_turned.at(g, 2))
                    a_hi.on(nc.scalar.copy(a_t[0][:, :], ring_a.bank("attT")[:, :]))
                elif s == "turn_quant":
                    act.wait_ge(a_turned.sem, a_turned.at(g, 3))
                    a_quantT.on(nc.scalar.copy(qxT[:, :], ring_a.bank("qxT")[:, :]))
                elif s[0] == "ffn":
                    def gate(j):
                        act.wait_ge(a_gate_up.sem, a_gate_up.at(g, 2 * j + 1))
                        act.wait_ge(a_scales.sem, a_scales.at(g))
                        if j >= 2:
                            act.wait_ge(a_gated.sem, a_gated.at(g, j - 1))
                        a_tanh.on(nc.scalar.activation(th[j % 2], ring_a.bank(("g", j))[:, :], ACT.Tanh,
                                                       scale=s_half[:, j:j + 1]))

                    j = s[1]
                    if s == ("ffn", 0, 0):
                        gate(0)
                    elif s[2]:
                        act.wait_ge(a_hturned.sem, a_hturned.at(g, j + 1))
                        a_hT.on(nc.scalar.copy(hqT[j % 2][:, :], ring_a.bank(("h", j))[:, :]))
                        if j + 1 < GB:
                            gate(j + 1)

            def b(g, s):
                if s == "norm":
                    act.wait_ge(ctxb_in.sem, ctxb_in.at(g, 16))
                    b_chi.on(nc.scalar.copy(b_c[0][:, :], cb[:, :]))
                elif s == "turn":
                    act.wait_ge(b_turned.sem, b_turned.at(g, 1))
                    b_hi.on(nc.scalar.copy(b_t[0][:, :], ring_b.bank("xT")[:, :]))
                elif s == "project":
                    for j in range(GB):
                        for n in range(2):
                            act.wait_ge(b_v_done.sem, b_v_done.at(g, 2 * j + n + 1))
                            b_v.on(nc.scalar.copy(v1[:, j, of(n, 8), 0:D1], ring_b.bank(("v", j, n))[:, :].rearrange(
                                "p (h d) -> p h d", d=D1)))
                elif s == "chunk_start":
                    for c in range(2):
                        query(g, c)
                    for h in range(2):
                        exp_b(g, h)
                elif s[0] == "chunk":
                    c, side = s[1:]
                    h = 2 * c + side
                    turned_in_b(g, h)
                    if side and c + 2 < C1:
                        query(g, c + 2)
                    if h + 2 < H:
                        exp_b(g, h + 2)
                    if side and c:
                        attended_hi(g, c - 1)
                elif s == "combine":
                    attended_hi(g, C1 - 1)
                    act.wait_ge(b_wout.sem, b_wout.at(g, C1))
                    b_gated_out.on(nc.scalar.activation(yT[:, :], sums_b[:, :], ACT.Identity,
                                                        bias=bo1_g[:, 0:1], scale=tanh_gate[:, 0:1]))
                elif s == "turn_x3":
                    act.wait_ge(b_turned.sem, b_turned.at(g, 3))
                    b_hi.on(nc.scalar.copy(b_t[0][:, :], ring_b.bank("x3T")[:, :]))
                elif s == "route":
                    act.wait_ge(b_lshift.sem, b_lshift.at(g))
                    b_lexp.on(nc.scalar.activation(lg[:, :, :], lg[:, :, :], ACT.Exp))
                elif s[0] == "expert":
                    n = s[1]

                    def gate(n):
                        act.wait_ge(b_g.sem, b_g.at(g, n + 1))
                        if n >= 2:
                            act.wait_ge(b_gated.sem, b_gated.at(g, n - 1))
                        b_tanh.on(nc.scalar.activation(tg[n % 2], ring_b.bank(("g", n))[:, :], ACT.Tanh, scale=0.5))

                    if s[2] == 0:
                        if n == 0:
                            act.wait_ge(b_cturned.sem, b_cturned.at(g))
                            b_cT.on(nc.scalar.copy(c3T[:, :], ring_b.bank("cT")[0:3 * E, 0:T // 2].bitcast(BF16)))
                            gate(0)
                        e = n // CE
                        if n % CE == CE - 1:
                            act.wait_ge(b_cspread.sem, b_cspread.at(g, e + 1))
                            if e >= 2:
                                act.wait_ge(b_ycomb.sem, b_ycomb.at(g, e - 1))
                            b_cin.on(nc.scalar.copy(c_b[e % 2], ring_b.bank(("c", e))[:, :]))
                        if n + 1 < NCH:
                            gate(n + 1)
                    else:
                        act.wait_ge(b_hidden.sem, b_hidden.at(g, n + 1))
                        if n >= 2:
                            act.wait_ge(b_y.sem, b_y.at(g, n - 1))
                        b_hhi.on(nc.scalar.copy(hp[n % 2][0][:, :], hf[n % 2]))

            run(act, a, b, set_up_round)

        @block.gpsimd
        def _(pool):
            def inverse_root(g, var, rstd, k, dst, src):
                pool.wait_ge(var.sem, var.at(g, k))
                rstd.on(nc.gpsimd.tensor_tensor(dst[:, :], src[:, :], minus_half[:, :], ALU.pow))

            pool.wait_ge(set_up, SET_UP)

            def weigh(g, u):
                pool.wait_ge(a_exp.sem, a_exp.at(g, u + 1))
                if u >= 2:
                    pool.wait_ge(a_gturned.sem, a_gturned.at(g, u - 1))
                j = u // NHG
                a_weighted.on(nc.gpsimd.tensor_tensor(
                    a_g[u % 2][:, :, :], a_p[u % 2][:, :, :], gp[:, j:j + 1, :].to_broadcast([P, HG, P]), ALU.mult))

            def a(g, s):
                if s == "norm":
                    inverse_root(g, a_var, a_rstd, 1, a_rs, a_ve)
                elif s == "quant":
                    inverse_root(g, a_var, a_rstd, 2, a_rs, a_ve)
                elif s == "attend_start":
                    pool.wait_ge(gp_in.sem, gp_in.at(g, 16))
                    for u in range(2):
                        weigh(g, u)
                elif s[0] == "attend" and s[1] + 2 < UNITS0:
                    weigh(g, s[1] + 2)

            def b(g, s):
                if s == "norm":
                    inverse_root(g, b_var, b_rstd, 1, b_rs, b_ve)
                    inverse_root(g, b_var, b_rstd, 2, b_rs, b_ve)
                elif s == "norm_x3":
                    inverse_root(g, b_var, b_rstd, 3, b_rs, b_ve)
                elif (s[0] == "expert" and s[2]) or s == "finish":
                    n = s[1] if s != "finish" else NCH + 1
                    e = (n - 1) // CE - 1
                    if n < NCH:
                        pool.wait_ge(b_hhi.sem, b_hhi.at(g, n + 1))
                        if n >= 2:
                            pool.wait_ge(b_y.sem, b_y.at(g, n - 1))
                        b_hlo.on(nc.gpsimd.tensor_tensor(hp[n % 2][1][:, :], hf[n % 2],
                                                         hp[n % 2][0][:, :].bitcast(F32), ALU.subtract))
                    if n % CE == 1 and e >= 1:
                        pool.wait_ge(b_ycomb.sem, b_ycomb.at(g, e + 1))
                        if e >= 2:
                            pool.wait_ge(b_acc.sem, b_acc.at(g, e - 1))
                        b_acc.on(nc.gpsimd.tensor_tensor(acc[:, :], acc[:, :], yc[e % 2], ALU.add))

            run(pool, a, b)

        @block.vector
        def _(dve):
            v = nc.vector
            tt, ts, stt = v.tensor_tensor, v.tensor_scalar, v.scalar_tensor_tensor

            steps_of = []

            def then(g, ins):
                step = steps_of[-1]
                step.on(ins)
                dve.wait_ge(step.sem, step.at(g, (step.made - 1) % step.n + 1))

            def wait(g, ev, k=1):
                dve.wait_ge(ev.sem, ev.at(g, k))

            v.memset(ones[:, :], 1.0)
            v.memset(minus_half[:, :], -0.5).then_inc(set_up, 1)
            dve.wait_ge(consts_in, 16 * N_CONSTANTS)
            v.tensor_copy(ident_b[:, :], ident[:, :])
            v.tensor_copy(expert_sel[:, :], expert_sel_f[:, :]).then_inc(set_up, 1)
            for n, ((_, w), src) in enumerate(zip(SMALL, small_at)):
                dve.wait_ge(hi_made, n + 1)
                tt(w[1][:, :], src, w[0][:, :].bitcast(F32), ALU.subtract)
            dve.wait_ge(f_in, 48)
            for n in range(3):
                last = v.tensor_reduce(f_sum[:, n:n + 1], f_at[n], AX_X, ALU.add, apply_absolute_value=True)
            last.then_inc(f_summed, 1)
            dve.wait_ge(f_total, 1)
            ts(f_mean[:, :], bank[0][:, 0:3], 1.0 / (P * F0), 1e-5, ALU.mult, ALU.max).then_inc(f_summed, 1)
            dve.wait_ge(f_summed, 2)
            v.reciprocal(f_inv[:, :], f_mean[:, :]).then_inc(f_summed, 1)
            ts(f_c[:, :], f_mean[:, :], 1.0 / 127.0, None, ALU.mult).then_inc(f_summed, 1)
            dve.wait_ge(f_summed, 4)
            ts(f_c[:, 0:1], f_c[:, 0:1], 0.5, None, ALU.mult)
            for step in range(3):
                for n, (_, w) in enumerate(FFN):
                    if step == 0:
                        last = ts(f_at[n], f_at[n], f_inv[:, n:n + 1], 1.0, ALU.mult, ALU.min)
                    elif step == 1:
                        last = ts(f_at[n], f_at[n], -1.0, MAGIC, ALU.max, ALU.add)
                    else:
                        last = ts(w[:, :], f_at[n], MAGIC, None, ALU.subtract)
                if step < 2:
                    last.then_inc(f_summed, 1)
                    dve.wait_ge(f_summed, 5 + step)
            def set_up_round(r):
                dve.wait_ge(round_hi, r + 1)
                tt(slots_of(r)[:, :, 1].rearrange("p c m n -> p c (m n)"),
                   round_in[r % 2][:, :, :, :].rearrange("p c m n -> p c (m n)"),
                   slots_of(r)[:, :, 0].rearrange("p c m n -> p c (m n)").bitcast(F32), ALU.subtract).then_inc(round_lo, 1)

            v.memset(f_sum[:, :], 0.0).then_inc(set_up, 1)

            def norm(g, dst, src, st, mv, ve, rs, xc, var, rstd, k, done):
                for j in range(GB):
                    v.bn_stats(st[:, j, :], src[:, j, :])
                dve.drain()
                for j in range(GB):
                    last = v.bn_aggr(mv[:, j, :], st[:, j, :])
                then(g, last)
                var.on(ts(ve[:, :], mv[:, :, 1], EPS, None, ALU.add))
                then(g, tt(xc[:, :, :], src[:, :, :], spread(mv[:, :, 0], P), ALU.subtract))
                wait(g, rstd, k)
                done(tt(dst[:, :, :], xc[:, :, :], spread(rs[:, :], P), ALU.mult))

            def low(g, pair_, unit, ring, hi, lo, k):
                wait(g, hi, k)
                lo.on(tt(pair_[1][:, :], ring.bank(unit)[:, :], pair_[0][:, :].bitcast(F32), ALU.subtract))

            def split3(g, dst, src, rest, done):
                then(g, v.tensor_copy(dst[0], src))
                then(g, tt(rest, src, dst[0], ALU.subtract))
                then(g, v.tensor_copy(dst[1], rest))
                done(tt(dst[2], rest, dst[1], ALU.subtract))

            def maxima(g, u, scored, ring, done, nm):
                wait(g, scored, u + 1)
                done.on(v.tensor_reduce(nm[:, u % 4, :], tiles(ring.bank(("S", u))[:, :]), AX_X, ALU.max, negate=True))

            def max_a(g, u):
                maxima(g, u, a_scored, ring_a, a_max, a_nm)

            def max_b(g, h):
                maxima(g, h, b_scored, ring_b, b_max, b_nm)

            def turned_in_a(g, u):
                wait(g, a_gturned, u + 1)
                if u >= 2:
                    wait(g, a_summed, u - 1)
                a_gT_in.on(v.tensor_copy(a_gT[u % 2][:, :], ring_a.bank(("T", u))[:, :]))

            def normalise_a(g, j):
                wait(g, a_summed, (j + 1) * NHG)
                then(g, v.reciprocal(a_rd[:, :], a_sum[:, j % 2, :]))
                a_attended.on(tt(att[:, j, :].rearrange("p (h d) -> p h d", d=D0),
                                 values_a.rearrange("p (h d) -> p h d", d=D0), spread(a_rd[:, :], D0), ALU.mult))

            def down_in_a(g, j):
                then(g, ts(s_down[:, j:j + 1], mh[:, j:j + 1], f_c[:, 2:3], None, ALU.mult))
                wait(g, a_down, j + 1)
                a_out.on(stt(x2[:, j, :], values_a, s_down[:, j:j + 1], x1[:, j, :], ALU.mult, ALU.add))

            def a(g, s):
                steps_of.append(a_step)
                if s == "norm":
                    wait(g, x_in, 16)
                    norm(g, a_n, xa, a_st, a_mv, a_ve, a_rs, a_xc, a_var, a_rstd, 1, a_normed.on)
                elif s == "turn":
                    wait(g, a_chi)
                    a_clo.on(tt(a_c[1][:, :], ca[:, :], a_c[0][:, :].bitcast(F32), ALU.subtract))
                    low(g, a_t, "xT", ring_a, a_hi, a_lo, 1)
                elif s == "project":
                    for n in range(2):
                        wait(g, a_qk, n + 1)
                        split3(g, [qk_3[n][:, c, :] for c in range(3)], qk_f[n], qk_r[:, :], a_split.on)
                    wait(g, a_projected, 3)
                    a_v.on(tt(va[:, :, :], tiles(ring_a.bank("v")[:, :]), over_tiles(bv_b[:, :]), ALU.add))
                    wait(g, mask_in, 16)
                    a_masks.on(ts(neg[:, :, :], mk[:, :, :], MASKED, -MASKED, ALU.mult, ALU.add))
                elif s == "attend_start":
                    for u in range(2):
                        max_a(g, u)
                elif s[0] == "attend":
                    u = s[1]
                    turned_in_a(g, u)
                    if u + 2 < UNITS0:
                        max_a(g, u + 2)
                    if u and u % NHG == 0:
                        normalise_a(g, u // NHG - 1)
                elif s == "combine":
                    normalise_a(g, GB - 1)
                    low(g, a_t, "attT", ring_a, a_hi, a_lo, 2)
                    wait(g, a_wo_done)
                    a_wo_read.on(tt(x1[:, :, :], tiles(ring_a.bank("wo")[:, :]), over_tiles(bo_b[:, :]), ALU.add))
                    wait(g, a_wo_read)
                    then(g, tt(x1[:, :, :], x1[:, :, :], xa[:, :, :], ALU.add))
                elif s == "quant":
                    norm(g, a_n, x1, a_st, a_mv, a_ve, a_rs, a_xc, a_var, a_rstd, 2, lambda i: then(g, i))
                    then(g, v.tensor_reduce(mx[:, :], a_n[:, :, :], AX_X, ALU.max, apply_absolute_value=True))
                    then(g, ts(mx[:, :], mx[:, :], 1e-5, None, ALU.max))
                    then(g, v.reciprocal(s127[:, :], mx[:, :]))
                    then(g, ts(s127[:, :], s127[:, :], 127.0, None, ALU.mult))
                    then(g, tt(qx[:, :, :], a_n[:, :, :], spread(s127[:, :], P), ALU.mult))
                    then(g, ts(qx[:, :, :], qx[:, :, :], 127.0, -128.0, ALU.min, ALU.max))
                    then(g, ts(qx[:, :, :], qx[:, :, :], MAGIC, None, ALU.add))
                    a_quant.on(ts(qx[:, :, :], qx[:, :, :], MAGIC, None, ALU.subtract))
                    ts(s_half[:, :], mx[:, :], f_c[:, 0:1], None, ALU.mult)
                    then(g, ts(s_up[:, :], mx[:, :], f_c[:, 1:2], None, ALU.mult))
                    a_scales.on(tt(s_both[:, :], s_half[:, :], s_up[:, :], ALU.mult))
                elif s[0] == "ffn" and s[2] == 0:
                    j = s[1]
                    h = hid[j % 2]
                    wait(g, a_tanh, j + 1)
                    if j >= 2:
                        wait(g, a_hturned, j - 1)
                    a_gated.on(stt(h, th[j % 2], 1.0, ring_a.bank(("g", j))[:, :], ALU.add, ALU.mult))
                    wait(g, a_gated, j + 1)
                    wait(g, a_gate_up, 2 * j + 2)
                    if j == 0:
                        wait(g, a_scales)
                    a_hidden.on(stt(h, h, s_both[:, j:j + 1], ring_a.bank(("u", j))[:, :], ALU.mult, ALU.mult))
                    wait(g, a_hidden, j + 1)
                    m, s127_ = mh[:, j:j + 1], h127[:, j:j + 1]
                    then(g, v.tensor_reduce(m, h, AX_X, ALU.max, apply_absolute_value=True))
                    then(g, ts(m, m, 1e-5, None, ALU.max))
                    then(g, v.reciprocal(s127_, m))
                    then(g, ts(s127_, s127_, 127.0, None, ALU.mult))
                    then(g, ts(h, h, s127_, 127.0, ALU.mult, ALU.min))
                    then(g, ts(h, h, -128.0, MAGIC, ALU.max, ALU.add))
                    a_hquant.on(ts(h, h, MAGIC, None, ALU.subtract))
                    if j:
                        down_in_a(g, j - 1)
                elif s == ("ffn", GB - 1, 1):
                    down_in_a(g, GB - 1)

            def key(g, c):
                wait(g, b_k_done, c + 1)
                b_k.on(v.tensor_copy(k1T[c % 2], ring_b.bank(("K", c))[:, :]))

            def attended_lo(g, c):
                wait(g, b_ahi, c + 1)
                b_alo.on(tt(hp[c % 2][1][:, :], ring_b.bank(("A", c))[:, :], hp[c % 2][0][:, :].bitcast(F32),
                            ALU.subtract))

            def normalise_b(g, h):
                wait(g, b_exp, h + 1)
                then(g, v.reciprocal(b_rd[:, h % 4, :], b_sum[:, h % 4, :]))
                wait(g, b_summed, h + 1)
                b_attended.on(tt(att1[h // 2 % 2][:, :, of(h % 2, D1)],
                                 values_b.rearrange("p (j d) -> p j d", d=D1), spread(b_rd[:, h % 4, :], D1), ALU.mult))

            def b(g, s):
                steps_of.append(b_step)
                if s == "norm":
                    wait(g, a_out, GB)
                    then(g, v.tensor_copy(xb[:, :, :], x2[:, :, :]))
                    norm(g, b_n, xb, b_st, b_mv, b_ve, b_rs, b_xc, b_var, b_rstd, 1, lambda i: then(g, i))
                    norm(g, b_n, b_n, b_st, b_mv, b_ve, b_rs, b_xc, b_var, b_rstd, 2, lambda i: then(g, i))
                    then(g, tt(b_n[:, :, :], b_n[:, :, :], over_tiles(gamma_b[:, :]), ALU.mult))
                    b_normed.on(tt(b_n[:, :, :], b_n[:, :, :], over_tiles(beta_b[:, :]), ALU.add))
                elif s == "turn":
                    wait(g, b_chi)
                    b_clo.on(tt(b_c[1][:, :], cb[:, :], b_c[0][:, :].bitcast(F32), ALU.subtract))
                    low(g, b_t, "xT", ring_b, b_hi, b_lo, 1)
                elif s == "chunk_start":
                    for c in range(2):
                        key(g, c)
                    for h in range(2):
                        max_b(g, h)
                elif s[0] == "chunk":
                    c, side = s[1:]
                    h = 2 * c + side
                    if side and c + 2 < C1:
                        key(g, c + 2)
                    if h + 2 < H:
                        max_b(g, h + 2)
                    if h:
                        normalise_b(g, h - 1)
                    if side and c:
                        attended_lo(g, c - 1)
                elif s == "combine":
                    normalise_b(g, H - 1)
                    attended_lo(g, C1 - 1)
                elif s == "turn_out":
                    wait(g, b_turned, 2)
                    b_x3.on(tt(x3[:, :, :], tiles(ring_b.bank("x3")[:, :]), xb[:, :, :], ALU.add))
                    wait(g, b_x3)
                elif s == "norm_x3":
                    norm(g, b_n, x3, b_st, b_mv, b_ve, b_rs, b_xc, b_var, b_rstd, 3, b_normed.on)
                elif s == "turn_x3":
                    low(g, b_t, "x3T", ring_b, b_hi, b_lo, 2)
                elif s == "route":
                    wait(g, b_logits)
                    logits = ring_b.bank("lg")[:, 0:GB * E].rearrange("p (j e) -> p j e", e=E)
                    then(g, v.tensor_reduce(red[:, :], logits, AX_X, ALU.max))
                    b_lshift.on(tt(lg[:, :, :], logits, spread(red[:, :], E), ALU.subtract))
                    wait(g, b_lexp)
                    then(g, v.tensor_reduce(red[:, :], lg[:, :, :], AX_X, ALU.add))
                    then(g, v.reciprocal(red2[:, :], red[:, :]))
                    then(g, tt(lg[:, :, :], lg[:, :, :], spread(red2[:, :], E), ALU.mult))
                    mine = lg[:, :, :].unsqueeze(3).to_broadcast([P, GB, E, E])
                    others = lg[:, :, :].unsqueeze(2).to_broadcast([P, GB, E, E])
                    tt(above[:, :, :, :], others, mine, ALU.is_gt)
                    then(g, tt(same[:, :, :, :], others, mine, ALU.is_equal))
                    then(g, tt(same[:, :, :, :].rearrange("p j e f -> p j (e f)"),
                               same[:, :, :, :].rearrange("p j e f -> p j (e f)"), over_tiles(lt[:, :]), ALU.mult))
                    then(g, tt(above[:, :, :, :], above[:, :, :, :], same[:, :, :, :], ALU.add))
                    then(g, v.tensor_reduce(sel[:, :, :], above[:, :, :, :], AX_X, ALU.add))
                    then(g, ts(sel[:, :, :], sel[:, :, :], TOPK - 0.5, None, ALU.is_lt))
                    then(g, tt(cw[:, :, :], sel[:, :, :], lg[:, :, :], ALU.mult))
                    then(g, v.tensor_reduce(red[:, :], cw[:, :, :], AX_X, ALU.add))
                    then(g, v.reciprocal(red2[:, :], red[:, :]))
                    then(g, tt(cw[:, :, :], cw[:, :, :], spread(red2[:, :], E), ALU.mult))
                    split3(g, [c3[:, :, c, :] for c in range(3)], cw[:, :, :], cr[:, :, :], b_combine.on)
                elif (s[0] == "expert" and s[2] == 0) or s == "finish":
                    n = s[1] if s != "finish" else NCH + 1
                    if n < NCH:
                        h = hf[n % 2]
                        wait(g, b_tanh, n + 1)
                        if n >= 2:
                            wait(g, b_hlo, n - 1)
                        b_gated.on(stt(h, tg[n % 2], 1.0, ring_b.bank(("g", n))[:, :], ALU.add, ALU.mult))
                        wait(g, b_gated, n + 1)
                        wait(g, b_u, n + 1)
                        b_hidden.on(stt(h, h, 0.5, ring_b.bank(("u", n))[:, :], ALU.mult, ALU.mult))
                    e = (n - 1) // CE - 1
                    if n % CE == 1 and e >= 0:
                        wait(g, b_y, n - 1)
                        wait(g, b_cin, e + 1)
                        if e >= 3:
                            wait(g, b_acc, e - 2)
                        b_ycomb.on(tt(yc[e % 2] if e else acc[:, :], sums_b[:, :], c_b[e % 2], ALU.mult))
                    if s == "finish":
                        wait(g, b_turned, 4)
                        b_out.on(tt(xo[:, :, :], tiles(ring_b.bank("fin")[:, :]), x3[:, :, :], ALU.add))

            run(dve, a, b, set_up_round)

        for name, e in events.items():
            assert e.made == 2 * e.n, (name, e.made, e.n)


def kernel(**inputs):
    import numpy as np
    import concourse.bacc as bacc
    from concourse.bass_utils import run_bass_kernel_spmd

    a = {k: np.asarray(v) for k, v in inputs.items()}
    turned = lambda m: m.swapaxes(-1, -2)
    column = lambda w: w.reshape(-1, 1)
    row = lambda w: w.reshape(1, -1)
    kv = a["L1_xattn_w_kv"]
    expert_selector = np.zeros((3, E, E, P), np.float32)
    expert_selector[:, np.arange(E), np.arange(E)] = 1
    arrays = {
        "x": a["x"],
        "ctxT": a["ctx_1024"].reshape(NB * P, P).T,
        "gp": a["fside_BxSxS2_0"],
        "mask": a["mask_BxSxS2_ik1"],
        "wq": a["L0_xattn_wq_k"], "bq": column(a["L0_xattn_wq_b"]),
        "wk": a["L0_xattn_wk_k"], "bk": column(a["L0_xattn_wk_b"]),
        "wv": a["L0_xattn_wv_k"], "bv": row(a["L0_xattn_wv_b"]),
        "wo": a["L0_xattn_wo_k"], "bo": row(a["L0_xattn_wo_b"]),
        "fwgT": a["L0_ffn_w_gate"].T,
        "fwuT": a["L0_ffn_w_up"].T,
        "fwdT": a["L0_ffn_w_down"].T.reshape(CF, P, P).transpose(1, 0, 2).reshape(P, F0),
        "gamma": row(a["L1_xattn_ln_gamma"]), "beta": row(a["L1_xattn_ln_beta"]),
        "wv1": kv[:, INNER1:],
        "bout1": column(a["L1_xattn_b_out"]), "gate": a["L1_xattn_gate"].reshape(1, 1),
        "routerT": a["L1_ffn_router_w"].T,
        "chunks": np.stack([
            np.concatenate([m.reshape(P, C1, P).transpose(1, 0, 2), n.T.reshape(P, NCH, P).transpose(1, 0, 2)])
            for m, n in ((a["L1_xattn_w_q"], a["L1_ffn_w_gate"].reshape(E * HID, P)),
                         (kv[:, :INNER1], a["L1_ffn_w_up"].reshape(E * HID, P)))]
            + [np.concatenate([a["L1_xattn_w_out"].reshape(C1, P, P),
                               turned(a["L1_ffn_w_down"]).reshape(NCH, P, P)])], axis=2).reshape(
                                   C1 + NCH, P, 3 * P),
        "identity": np.eye(P, dtype=np.float32),
        "expert_selector": expert_selector.reshape(3 * E, E * P),
        "earlier": np.tril(np.ones((E, E), np.float32), -1).reshape(1, E * E),
    }
    arrays = {k + "_dram": np.ascontiguousarray(w) for k, w in arrays.items()}
    nc = bacc.Bacc("TRN2", target_bir_lowering=False, num_devices=1)
    args = [nc.dram_tensor(k, w.shape, mybir.dt.from_np(w.dtype), kind="ExternalInput").ap()
            for k, w in arrays.items()]
    out = nc.dram_tensor("out_dram", (NB, P, P), F32, kind="ExternalOutput").ap()
    two_layers(nc, *args, out)
    result = run_bass_kernel_spmd(nc, [arrays], core_ids=[0])
    return result.results[0]["out_dram"]
```
